# Optimizing a Trainium2 kernel written in Bass

```python
import numpy as np
import jax
import jax.numpy as jnp

def _softmax(x, axis=-1):
    return jax.nn.softmax(x, axis=axis)

def _gelu(x):
    return jax.nn.gelu(x, approximate=True)

def _silu(x):
    return jax.nn.silu(x)

def _sigmoid(x):
    return jax.nn.sigmoid(x)

def _layernorm(x, axis=-1, eps=1e-05):
    m = jnp.mean(x, axis=axis, keepdims=True)
    v = jnp.var(x, axis=axis, keepdims=True)
    return (x - m) / jnp.sqrt(v + eps)

def _scatter_add(tgt, idx, src, axis=0):
    return tgt.at[idx].add(src)

def _segment_sum(src, seg, n):
    return jax.ops.segment_sum(src, seg, n)
kernel_name = 'mk_dlrm_tower_d1_rec_r8_782db6'

def setup_inputs(seed: int=0):
    np.random.seed(seed)
    _w = jnp.asarray

    def _rec_inputs():
        import jax
        import jax.numpy as jnp
        _tk = jax.random.key(seed)
        dense_ctx = jax.random.normal(jax.random.fold_in(_tk, 190), (2048, 16), jnp.float32)
        ids = jnp.stack([jax.random.randint(jax.random.fold_in(_tk, 200 + f), (2048,), 0, v, jnp.int32) for f, v in enumerate([125000, 1000, 1000, 1250, 12500, 1000, 1250, 12500, 1250, 1000, 12500, 1250, 125000, 125000, 12500, 12500, 1000, 12500, 1000, 1250, 1000, 12500, 12500, 1250, 1000, 1250, 1000, 1000, 1000, 1250, 1000, 1250])], axis=1)
        tbl_0 = 0.05 * jax.random.normal(jax.random.fold_in(_tk, 500 + 0), (125000, 64), jnp.float32)
        tbl_1 = 0.05 * jax.random.normal(jax.random.fold_in(_tk, 500 + 1), (1000, 64), jnp.float32)
        tbl_2 = 0.05 * jax.random.normal(jax.random.fold_in(_tk, 500 + 2), (1000, 64), jnp.float32)
        tbl_3 = 0.05 * jax.random.normal(jax.random.fold_in(_tk, 500 + 3), (1250, 64), jnp.float32)
        tbl_4 = 0.05 * jax.random.normal(jax.random.fold_in(_tk, 500 + 4), (12500, 64), jnp.float32)
        tbl_5 = 0.05 * jax.random.normal(jax.random.fold_in(_tk, 500 + 5), (1000, 64), jnp.float32)
        tbl_6 = 0.05 * jax.random.normal(jax.random.fold_in(_tk, 500 + 6), (1250, 64), jnp.float32)
        tbl_7 = 0.05 * jax.random.normal(jax.random.fold_in(_tk, 500 + 7), (12500, 64), jnp.float32)
        tbl_8 = 0.05 * jax.random.normal(jax.random.fold_in(_tk, 500 + 8), (1250, 64), jnp.float32)
        tbl_9 = 0.05 * jax.random.normal(jax.random.fold_in(_tk, 500 + 9), (1000, 64), jnp.float32)
        tbl_10 = 0.05 * jax.random.normal(jax.random.fold_in(_tk, 500 + 10), (12500, 64), jnp.float32)
        tbl_11 = 0.05 * jax.random.normal(jax.random.fold_in(_tk, 500 + 11), (1250, 64), jnp.float32)
        tbl_12 = 0.05 * jax.random.normal(jax.random.fold_in(_tk, 500 + 12), (125000, 64), jnp.float32)
        tbl_13 = 0.05 * jax.random.normal(jax.random.fold_in(_tk, 500 + 13), (125000, 64), jnp.float32)
        tbl_14 = 0.05 * jax.random.normal(jax.random.fold_in(_tk, 500 + 14), (12500, 64), jnp.float32)
        tbl_15 = 0.05 * jax.random.normal(jax.random.fold_in(_tk, 500 + 15), (12500, 64), jnp.float32)
        tbl_16 = 0.05 * jax.random.normal(jax.random.fold_in(_tk, 500 + 16), (1000, 64), jnp.float32)
        tbl_17 = 0.05 * jax.random.normal(jax.random.fold_in(_tk, 500 + 17), (12500, 64), jnp.float32)
        tbl_18 = 0.05 * jax.random.normal(jax.random.fold_in(_tk, 500 + 18), (1000, 64), jnp.float32)
        tbl_19 = 0.05 * jax.random.normal(jax.random.fold_in(_tk, 500 + 19), (1250, 64), jnp.float32)
        tbl_20 = 0.05 * jax.random.normal(jax.random.fold_in(_tk, 500 + 20), (1000, 64), jnp.float32)
        tbl_21 = 0.05 * jax.random.normal(jax.random.fold_in(_tk, 500 + 21), (12500, 64), jnp.float32)
        tbl_22 = 0.05 * jax.random.normal(jax.random.fold_in(_tk, 500 + 22), (12500, 64), jnp.float32)
        tbl_23 = 0.05 * jax.random.normal(jax.random.fold_in(_tk, 500 + 23), (1250, 64), jnp.float32)
        tbl_24 = 0.05 * jax.random.normal(jax.random.fold_in(_tk, 500 + 24), (1000, 64), jnp.float32)
        tbl_25 = 0.05 * jax.random.normal(jax.random.fold_in(_tk, 500 + 25), (1250, 64), jnp.float32)
        tbl_26 = 0.05 * jax.random.normal(jax.random.fold_in(_tk, 500 + 26), (1000, 64), jnp.float32)
        tbl_27 = 0.05 * jax.random.normal(jax.random.fold_in(_tk, 500 + 27), (1000, 64), jnp.float32)
        tbl_28 = 0.05 * jax.random.normal(jax.random.fold_in(_tk, 500 + 28), (1000, 64), jnp.float32)
        tbl_29 = 0.05 * jax.random.normal(jax.random.fold_in(_tk, 500 + 29), (1250, 64), jnp.float32)
        tbl_30 = 0.05 * jax.random.normal(jax.random.fold_in(_tk, 500 + 30), (1000, 64), jnp.float32)
        tbl_31 = 0.05 * jax.random.normal(jax.random.fold_in(_tk, 500 + 31), (1250, 64), jnp.float32)
        _rk = jax.random.fold_in(_tk, 7)
        W_top1 = 0.0428746 * jax.random.normal(jax.random.fold_in(_tk, 801), (544, 512), jnp.float32)
        W_top2 = 0.0441942 * jax.random.normal(jax.random.fold_in(_tk, 802), (512, 256), jnp.float32)
        W_top3 = 0.0625 * jax.random.normal(jax.random.fold_in(_tk, 803), (256, 1), jnp.float32)
        b_top1 = jnp.zeros((512,), jnp.float32)
        b_top2 = jnp.zeros((256,), jnp.float32)
        return (dense_ctx, ids, tbl_0, tbl_1, tbl_2, tbl_3, tbl_4, tbl_5, tbl_6, tbl_7, tbl_8, tbl_9, tbl_10, tbl_11, tbl_12, tbl_13, tbl_14, tbl_15, tbl_16, tbl_17, tbl_18, tbl_19, tbl_20, tbl_21, tbl_22, tbl_23, tbl_24, tbl_25, tbl_26, tbl_27, tbl_28, tbl_29, tbl_30, tbl_31, W_top1, b_top1, W_top2, b_top2, W_top3)
    dense_ctx, ids, tbl_0, tbl_1, tbl_2, tbl_3, tbl_4, tbl_5, tbl_6, tbl_7, tbl_8, tbl_9, tbl_10, tbl_11, tbl_12, tbl_13, tbl_14, tbl_15, tbl_16, tbl_17, tbl_18, tbl_19, tbl_20, tbl_21, tbl_22, tbl_23, tbl_24, tbl_25, tbl_26, tbl_27, tbl_28, tbl_29, tbl_30, tbl_31, W_top1, b_top1, W_top2, b_top2, W_top3 = _rec_inputs()

    def _L0_rec_setup():
        import jax, jax.numpy as jnp
        import numpy as np
        B, F, D = (512, 32, 64)
        II, JJ = np.triu_indices(F, k=1)
        P = II.shape[0]
        key = jax.random.key(seed)
        kx, kk = jax.random.split(key)
        x = jax.random.normal(kx, (B, F, D), dtype=jnp.float32)
        kernels = jax.random.normal(kk, (P, D, D), dtype=jnp.float32) * 0.001
        return {'x': x, 'kernels': kernels}
    _L0_rec_all = _L0_rec_setup()
    _L0_rec_in = {k: v for k, v in _L0_rec_all.items() if k in ('kernels',)}
    del _L0_rec_all
    return {'dense_ctx': dense_ctx, 'ids': ids, 'tbl_0': tbl_0, 'tbl_1': tbl_1, 'tbl_2': tbl_2, 'tbl_3': tbl_3, 'tbl_4': tbl_4, 'tbl_5': tbl_5, 'tbl_6': tbl_6, 'tbl_7': tbl_7, 'tbl_8': tbl_8, 'tbl_9': tbl_9, 'tbl_10': tbl_10, 'tbl_11': tbl_11, 'tbl_12': tbl_12, 'tbl_13': tbl_13, 'tbl_14': tbl_14, 'tbl_15': tbl_15, 'tbl_16': tbl_16, 'tbl_17': tbl_17, 'tbl_18': tbl_18, 'tbl_19': tbl_19, 'tbl_20': tbl_20, 'tbl_21': tbl_21, 'tbl_22': tbl_22, 'tbl_23': tbl_23, 'tbl_24': tbl_24, 'tbl_25': tbl_25, 'tbl_26': tbl_26, 'tbl_27': tbl_27, 'tbl_28': tbl_28, 'tbl_29': tbl_29, 'tbl_30': tbl_30, 'tbl_31': tbl_31, 'W_top1': W_top1, 'b_top1': b_top1, 'W_top2': W_top2, 'b_top2': b_top2, 'W_top3': W_top3, 'L0_rec_kernels': _L0_rec_in['kernels']}

def reference(dense_ctx, ids, tbl_0, tbl_1, tbl_2, tbl_3, tbl_4, tbl_5, tbl_6, tbl_7, tbl_8, tbl_9, tbl_10, tbl_11, tbl_12, tbl_13, tbl_14, tbl_15, tbl_16, tbl_17, tbl_18, tbl_19, tbl_20, tbl_21, tbl_22, tbl_23, tbl_24, tbl_25, tbl_26, tbl_27, tbl_28, tbl_29, tbl_30, tbl_31, W_top1, b_top1, W_top2, b_top2, W_top3, L0_rec_kernels):
    import jax
    import jax.numpy as jnp

    def _L0_rec_ref(x, kernels):
        import jax, jax.numpy as jnp
        import numpy as np
        B, F, D = (512, 32, 64)
        II, JJ = np.triu_indices(F, k=1)
        P = II.shape[0]
        z = jnp.sum(x, axis=-1)
        xi = x[:, II, :]
        xj = x[:, JJ, :]
        outer = jnp.einsum('bpd,pde,bpe->bp', xi, kernels, xj)
        return jnp.concatenate([z, outer], axis=1)
    e = jnp.stack([tbl_0[ids[:, 0]], tbl_1[ids[:, 1]], tbl_2[ids[:, 2]], tbl_3[ids[:, 3]], tbl_4[ids[:, 4]], tbl_5[ids[:, 5]], tbl_6[ids[:, 6]], tbl_7[ids[:, 7]], tbl_8[ids[:, 8]], tbl_9[ids[:, 9]], tbl_10[ids[:, 10]], tbl_11[ids[:, 11]], tbl_12[ids[:, 12]], tbl_13[ids[:, 13]], tbl_14[ids[:, 14]], tbl_15[ids[:, 15]], tbl_16[ids[:, 16]], tbl_17[ids[:, 17]], tbl_18[ids[:, 18]], tbl_19[ids[:, 19]], tbl_20[ids[:, 20]], tbl_21[ids[:, 21]], tbl_22[ids[:, 22]], tbl_23[ids[:, 23]], tbl_24[ids[:, 24]], tbl_25[ids[:, 25]], tbl_26[ids[:, 26]], tbl_27[ids[:, 27]], tbl_28[ids[:, 28]], tbl_29[ids[:, 29]], tbl_30[ids[:, 30]], tbl_31[ids[:, 31]]], axis=1)
    z = _L0_rec_ref(e, L0_rec_kernels)
    z = z.reshape(z.shape[0], -1)
    h = jnp.concatenate([z, dense_ctx], axis=1)
    h = jnp.maximum(h @ W_top1 + b_top1, 0.0)
    h = jnp.maximum(h @ W_top2 + b_top2, 0.0)
    y = h @ W_top3
    return y

_drawn_inputs = setup_inputs


def setup_inputs(seed=0):
    import zlib

    import numpy as np

    out = dict(_drawn_inputs(seed))
    spreads = {'b_top1': (0.0, 0.1), 'b_top2': (0.0, 0.1)}
    factors = {'L0_rec_kernels': 64.0}
    for name, (base, spread) in spreads.items():
        noise = np.random.default_rng([zlib.crc32(name.encode()), seed]).standard_normal(out[name].shape)
        drawn = base * np.exp(spread * noise) if base else spread * noise
        out[name] = jnp.asarray(drawn.astype(out[name].dtype))
    for name, factor in factors.items():
        out[name] = (out[name] * factor).astype(out[name].dtype)
    return out
```

```python
from contextlib import ExitStack

import concourse.bass as bass
from concourse import mybir

B, F, D = 2048, 32, 64
DENSE, H1, H2 = 16, 512, 256
HALVES = 2
HB = B // HALVES
NB = 512
CH = HB // NB
TILES = HB // 128
STAGES = F // 2
MR = 3
PR = 5
P = 128


def pair_index(i, j):
    return i * F - i * (i + 1) // 2 + j - i - 1


def make_slots():
    slots = []
    for s in range(F):
        i = F - 1 - s
        slots.append((s, None))
        slots += [(s, m) for m in range(F // 2 - 1, (i + 1) // 2 - 1, -1)]
    return slots


SLOTS = make_slots()
NS = len(SLOTS)
UNITS = [(s, m) for s, m in SLOTS if m is not None]
NU = len(UNITS)
UNIT_OF = {}
SLOT_OF = []
for _k, (_s, _m) in enumerate(SLOTS):
    if _m is not None:
        UNIT_OF[_k] = len(SLOT_OF)
        SLOT_OF.append(_k)
FIRST = [SLOTS.index((s, None)) for s in range(F)]
UNITS_UPTO = [sum(1 for s, _ in UNITS if s <= t) for t in range(F)]
BLOCK = 32
BLOCKS = NS // BLOCK
ZROWS = 2 * NS
ZIN = ZROWS + DENSE
KC = (ZIN + P - 1) // P
KLAST = ZIN - (KC - 1) * P
KB = 4
KBATCH = NU // KB
KLEAD = 2
KLOAD = 3
REDUCES = NS // 2

AHEAD = 2
STAGE_AT = {FIRST[2 * a - 1 - (a >= 8) - (a >= 11)]: a for a in range(AHEAD, STAGES)}
assert len(STAGE_AT) == STAGES - AHEAD
STACK_AT = {}
for _k, _a in STAGE_AT.items():
    for _s in (2 * _a, 2 * _a + 1):
        STACK_AT.setdefault(max(_k, FIRST[_s - 3]), []).append(_s)
NEXT_AT = {226: 0, 242: 1}
NEXT_SPLIT_AT = {228: 0, FIRST[30] + 3: 1}
NEXT_STACK_AT = {FIRST[29]: 0, FIRST[30]: 1, FIRST[31]: 2}


def k_batches(h, k, lead):
    if k not in UNIT_OF or UNIT_OF[k] % KB:
        return ()
    g = h * KBATCH + UNIT_OF[k] // KB + lead
    return (g,) if g < HALVES * KBATCH else ()


def units_upto(h, s):
    h, s = (h, s) if s >= 0 else (h - 1, s + F)
    return h * NU + UNITS_UPTO[s] if h >= 0 else 0


def reduces_upto(h, k):
    return max(0, (h * NS + k) // 2 + 1)


def reduces_of_unit(g):
    return reduces_upto(g // NU, SLOT_OF[g % NU])


def z_row(k, t):
    b, kk = divmod(k, BLOCK)
    return b * 2 * BLOCK + (kk % 2) * BLOCK + 2 * (kk // 2) + t


def dlrm_tower(nc, ids, tables, kmat, dense_t, w1, b1, w2, b2, w3, out):
    fp32, fp32r, i32 = mybir.dt.float32, mybir.dt.float32r, mybir.dt.int32
    ALU = mybir.AluOpType
    ACT = mybir.ActivationFunctionType

    z_dram = nc.dram_tensor("z_scratch", (ZROWS, B), fp32).ap()

    ctx = ExitStack()
    with ctx:
        def sb(name, shape, dt=fp32):
            return ctx.enter_context(nc.sbuf_tensor(name, shape, dt))

        def pb(name, shape, dt=fp32):
            return ctx.enter_context(nc.psum_tensor(name, shape, dt))

        def sem(name):
            return ctx.enter_context(nc.semaphore(name))

        x_t = sb("x_t", [P, HALVES, STAGES, HB])
        idx = sb("idx", [P, F * TILES], i32)
        gathered = sb("gathered", [P, 2, TILES, 2, D])
        x_high = sb("x_high", [P, HB], fp32r)
        x_low = sb("x_low", [P, HB], fp32r)
        x_split = sb("x_split", [P, 4, HB], fp32r)
        k_raw = sb("k_raw", [P, 2, KB * P])
        k_high = sb("k_high", [P, 4, KB * P], fp32r)
        k_low = sb("k_low", [P, 4, KB * P], fp32r)
        prod = sb("prod", [P, PR, HB])
        z_out = sb("z_out", [P, 2, NB])
        ident = sb("ident", [P, P])
        sel = sb("sel", [P, 2 * BLOCK - 2])
        b1_sb = sb("b1_sb", [P, H1 // P])
        b2_sb = sb("b2_sb", [P, H2 // P])
        w3_sb = sb("w3_sb", [P, H2 // P])

        room = x_t[:, 0, :, :].rearrange("p a b -> p (a b)")
        at = [0]

        def take(n):
            at[0] += n
            assert at[0] <= STAGES * HB
            return room[:, at[0] - n:at[0]]

        w1_sb = take(KC * H1).rearrange("p (k n) -> p k n", k=KC)
        w2_sb = take(H1 // P * H2).rearrange("p (k n) -> p k n", k=H1 // P)
        z_sb = take(2 * KC * NB).rearrange("p (r k n) -> p r k n", r=2, k=KC)
        h1_sb = take(2 * (H1 // P) * NB).rearrange("p (r k n) -> p r k n", r=2, k=H1 // P)
        h2_sb = take(2 * (H2 // P) * NB).rearrange("p (r k n) -> p r k n", r=2, k=H2 // P)

        y_sb = gathered[0:1, :, :, :, :].rearrange("p a t f d -> p (a t f d)")[:, 0:B]

        m_ps = pb("m_ps", [P, MR, HB])
        acc = pb("acc", [P, NB])
        tr = pb("tr", [P, NB])

        consts_ready = sem("consts_ready")
        zeroed = sem("zeroed")
        sel_zeroed = sem("sel_zeroed")
        idx_loaded = sem("idx_loaded")
        stage_gathered = [sem(f"stage_gathered{r}") for r in range(2)]
        transposed = sem("transposed")
        xt_ready = sem("xt_ready")
        split_loaded = [sem(f"split_loaded{r}") for r in range(4)]
        x_high_ready = sem("x_high_ready")
        x_ready = sem("x_ready")
        k_loaded = [sem(f"k_loaded{r}") for r in range(2)]
        k_high_ready = sem("k_high_ready")
        k_ready = sem("k_ready")
        unit_done = sem("unit_done")
        prod_ready = sem("prod_ready")
        reduced = sem("reduced")
        z_ready = sem("z_ready")
        z_stored = [sem(f"z_stored{r}") for r in range(2)]
        small_loaded = sem("small_loaded")
        weights_loaded = sem("weights_loaded")
        z_loaded = [sem(f"z_loaded{r}") for r in range(2)]
        h1_ready = sem("h1_ready")
        h2_ready = sem("h2_ready")
        y_summed = sem("y_summed")
        y_ready = sem("y_ready")
        y_stored = sem("y_stored")

        STAGE_INCS = (STAGES // 2) * 2 * TILES * 16
        MLP = B // NB
        STORES = [len(range(r, BLOCKS, 2)) for r in range(2)]

        h1_summed = sem("h1_summed")
        h2_summed = sem("h2_summed")

        def h1_ps(c, n):
            return m_ps[:, n // 2, (n % 2) * NB:(n % 2 + 1) * NB]

        def h2_ps(c, n):
            return m_ps[:, 2, n * NB:(n + 1) * NB]

        def y_ps(c):
            return tr[0:1, :]

        block = ctx.enter_context(nc.Block())

        @block.gpsimd
        def _(pool):
            nc.gpsimd.memset(ident[:], 0.0).then_inc(zeroed, 1)
            pool.wait_ge(zeroed, 1)
            nc.gpsimd.affine_select(out=ident[:], in_=ident[:], compare_op=ALU.not_equal, fill=1.0,
                                    base=0, pattern=[[-1, P]], channel_multiplier=1).then_inc(consts_ready, 1)

            def load_ids(h, after):
                for r in range(2) if after else ():
                    pool.wait_ge(stage_gathered[r], h * STAGE_INCS)
                pool.dma_start(idx[:], ids[h, :, :]).then_inc(idx_loaded, 16)
                pool.wait_ge(idx_loaded, 16 * h + 16)

            def gather(h, a, first=False):
                if not first:
                    pool.wait_ge(transposed, (h * STAGES + a - 1) * CH)
                for t in range(TILES):
                    for f in range(2):
                        field = 2 * (STAGES - 1 - a) + f
                        col = (2 * a + f) * TILES + t
                        nc.gpsimd.indirect_dma_start(
                            out=gathered[:, a % 2, t, f, :], out_offset=None, in_=tables[field],
                            in_offset=bass.IndirectOffsetOnAxis(ap=idx[:, col:col + 1], axis=0),
                        ).then_inc(stage_gathered[a % 2], 16)

            load_ids(0, False)
            for a in range(AHEAD):
                gather(0, a, first=True)
            for h in range(HALVES):
                for a in range(AHEAD, STAGES):
                    gather(h, a)
                if h < HALVES - 1:
                    load_ids(h + 1, True)
                    for a in range(AHEAD):
                        gather(h + 1, a)

        @block.sync
        def _(sp):
            sp.dma_start(b1_sb[:], b1).then_inc(small_loaded, 16)
            sp.dma_start(b2_sb[:], b2).then_inc(small_loaded, 16)
            sp.dma_start(w3_sb[:], w3).then_inc(small_loaded, 16)

            def load_weights():
                sp.wait_ge(x_ready, STAGES)
                sp.wait_ge(prod_ready, NU)
                sp.dma_start(w1_sb[:, 0:KC - 1, :], w1[0:(KC - 1) * P, :].rearrange("(k p) n -> p k n", p=P)).then_inc(weights_loaded, 16)
                sp.dma_start(w1_sb[0:KLAST, KC - 1, :], w1[(KC - 1) * P:ZIN, :]).then_inc(weights_loaded, 16)
                sp.dma_start(w2_sb, w2.rearrange("(k p) n -> p k n", p=P)).then_inc(weights_loaded, 16)

            def load_z(c):
                if c >= 2:
                    sp.wait_ge(h1_summed, (c - 1) * (H1 // P))
                if c % CH == 0:
                    for r in range(2):
                        sp.wait_ge(z_stored[r], (c // CH + 1) * STORES[r] * 64)
                cols = slice(c * NB, (c + 1) * NB)
                sp.dma_start(z_sb[:, c % 2, 0:KC - 1, :],
                             z_dram[0:(KC - 1) * P, cols].rearrange("(k p) n -> p k n", p=P)).then_inc(z_loaded[c % 2], 16)
                sp.dma_start(z_sb[0:KLAST - DENSE, c % 2, KC - 1, :], z_dram[(KC - 1) * P:ZROWS, cols]).then_inc(z_loaded[c % 2], 16)
                sp.dma_start(z_sb[KLAST - DENSE:KLAST, c % 2, KC - 1, :], dense_t[:, cols]).then_inc(z_loaded[c % 2], 16)

            for h in range(HALVES):
                def load_k(g):
                    if g >= 2:
                        sp.wait_ge(k_ready, g - 1)
                    kb = g % KBATCH
                    for half in range(2):
                        sp.dma_start(k_raw[half * D:half * D + D, g % 2, :],
                                     kmat[:, kb * KB * P:(kb + 1) * KB * P]).then_inc(k_loaded[g % 2], 16)

                def stack_x(h, s):
                    i, a = F - 1 - s, s // 2
                    if h or s >= 4:
                        sp.wait_ge(unit_done, units_upto(h, s - 4))
                        sp.wait_ge(reduced, reduces_upto(h, FIRST[s - 4] - (NS if s < 4 else 0)))
                    sp.wait_ge(x_ready, h * STAGES + a + 1)
                    lo = (i % 2) * D
                    sp.dma_start(x_split[0:D, s % 4, :].bitcast(fp32), x_high[lo:lo + D, :].bitcast(fp32)).then_inc(split_loaded[s % 4], 16)
                    sp.dma_start(x_split[D:P, s % 4, :].bitcast(fp32), x_low[lo:lo + D, :].bitcast(fp32)).then_inc(split_loaded[s % 4], 16)

                def store_z(b):
                    sp.wait_ge(z_ready, h * BLOCKS + b + 1)
                    for g in range(4):
                        row = b * 2 * BLOCK + (g // 2) * BLOCK
                        sp.dma_start(z_dram[row:row + BLOCK, bass.ds(h * HB + (g % 2) * NB, NB)],
                                     z_out[g * BLOCK:(g + 1) * BLOCK, b % 2, :]).then_inc(z_stored[b % 2], 16)

                if h == 0:
                    for kb in range(KLOAD):
                        load_k(kb)
                    for s in range(3):
                        stack_x(h, s)
                for k in range(NS):
                    if h and k == NS // 2:
                        load_weights()
                        load_z(0)
                        load_z(1)
                    if k == 0:
                        stack_x(h, 3)
                    for s in STACK_AT.get(k, ()):
                        stack_x(h, s)
                    if h < HALVES - 1 and k in NEXT_STACK_AT:
                        stack_x(h + 1, NEXT_STACK_AT[k])
                    for g in k_batches(h, k, KLOAD):
                        load_k(g)
                    if k % BLOCK == 6 and k > BLOCK:
                        store_z(k // BLOCK - 1)
                store_z(BLOCKS - 1)
            for c in range(2, MLP):
                load_z(c)
            sp.wait_ge(y_ready, MLP)
            sp.dma_start(out, y_sb).then_inc(y_stored, 16)
            sp.wait_ge(y_stored, 16)

        @block.scalar
        def _(act):
            def keep_xt(h, a):
                for c in range(CH):
                    act.wait_ge(transposed, (h * STAGES + a) * CH + c + 1)
                    nc.scalar.activation(x_t[:, h, a, c * NB:(c + 1) * NB], tr[:], ACT.Copy).then_inc(xt_ready, 1)

            for a in range(AHEAD):
                keep_xt(0, a)
            for h in range(HALVES):
                def split_k(g):
                    act.wait_ge(k_loaded[g % 2], 32 * (g // 2 + 1))
                    if g >= 4:
                        act.wait_ge(unit_done, KB * (g - 3))
                    nc.scalar.activation(k_high[:, g % 4, :], k_raw[:, g % 2, :], ACT.Copy).then_inc(k_high_ready, 1)

                def split_x(h, a):
                    for s in (2 * a - 2, 2 * a - 1) if h or a else ():
                        act.wait_ge(split_loaded[s % 4], h * (32 * F // 4) + (32 * (s // 4 + 1) if a else 0))
                    act.wait_ge(xt_ready, (h * STAGES + a + 1) * CH)
                    nc.scalar.activation(x_high[:], x_t[:, h, a, :], ACT.Copy).then_inc(x_high_ready, 1)

                def keep_z(b):
                    act.wait_ge(reduced, h * REDUCES + (b + 1) * BLOCK // 2)
                    if h or b >= 2:
                        act.wait_ge(z_stored[b % 2], h * (64 * STORES[b % 2]) + 64 * (b // 2))
                    nc.scalar.activation(z_out[:, b % 2, :], acc[:], ACT.Copy).then_inc(z_ready, 1)

                if h == 0:
                    split_x(h, 0)
                    for g in range(KLEAD):
                        split_k(g)
                    split_x(h, 1)
                for k in range(NS):
                    if k in STAGE_AT:
                        keep_xt(h, STAGE_AT[k])
                        split_x(h, STAGE_AT[k])
                    if h < HALVES - 1:
                        if k in NEXT_AT:
                            keep_xt(h + 1, NEXT_AT[k])
                        if k in NEXT_SPLIT_AT:
                            split_x(h + 1, NEXT_SPLIT_AT[k])
                    for g in k_batches(h, k, KLEAD):
                        split_k(g)
                    if k % BLOCK == 3 and k > BLOCK:
                        keep_z(k // BLOCK - 1)
                keep_z(BLOCKS - 1)
            act.wait_ge(small_loaded, 48)

            def keep_h1(c):
                if c >= 2:
                    act.wait_ge(h2_summed, (c - 1) * (H2 // P))
                for n in range(H1 // P):
                    act.wait_ge(h1_summed, c * (H1 // P) + n + 1)
                    last = nc.scalar.activation(h1_sb[:, c % 2, n, :], h1_ps(c, n), ACT.Relu,
                                                bias=b1_sb[:, n:n + 1])
                    last.then_inc(h1_ready, 1)

            def keep_h2(c):
                if c >= 2:
                    act.wait_ge(y_summed, c - 1)
                for n in range(H2 // P):
                    act.wait_ge(h2_summed, c * (H2 // P) + n + 1)
                    nc.scalar.activation(h2_sb[:, c % 2, n, :], h2_ps(c, n), ACT.Relu,
                                         bias=b2_sb[:, n:n + 1]).then_inc(h2_ready, 1)

            keep_h1(0)
            for c in range(MLP):
                if c + 1 < MLP:
                    keep_h1(c + 1)
                keep_h2(c)

        @block.vector
        def _(dve):
            nc.vector.memset(sel[:], 0.0).then_inc(sel_zeroed, 1)
            dve.wait_ge(sel_zeroed, 1)
            nc.vector.memset(sel[0:D, BLOCK - 2:BLOCK - 1], 1.0).then_inc(consts_ready, 1)
            nc.vector.memset(sel[D:P, BLOCK - 1:BLOCK], 1.0).then_inc(consts_ready, 1)
            for h in range(HALVES):
                def split_k(g):
                    dve.wait_ge(k_high_ready, g + 1)
                    nc.vector.tensor_tensor(k_low[:, g % 4, :], k_raw[:, g % 2, :],
                                            k_high[:, g % 4, :].bitcast(fp32), ALU.subtract).then_inc(k_ready, 1)

                def split_x(h, a):
                    dve.wait_ge(x_high_ready, h * STAGES + a + 1)
                    nc.vector.tensor_tensor(x_low[:], x_t[:, h, a, :],
                                            x_high[:].bitcast(fp32), ALU.subtract).then_inc(x_ready, 1)

                if h == 0:
                    split_x(h, 0)
                    for g in range(KLEAD):
                        split_k(g)
                    split_x(h, 1)
                for k in range(NS):
                    if k in UNIT_OF:
                        u, m = h * NU + UNIT_OF[k], SLOTS[k][1]
                        dve.wait_ge(unit_done, u + 1)
                        if u >= PR:
                            dve.wait_ge(reduced, reduces_of_unit(u - PR))
                        nc.vector.tensor_tensor(prod[:, u % PR, :], m_ps[:, u % MR, :],
                                                x_t[:, h, STAGES - 1 - m, :], ALU.mult).then_inc(prod_ready, 1)
                        for g in k_batches(h, k, KLEAD):
                            split_k(g)
                    if k in STAGE_AT:
                        split_x(h, STAGE_AT[k])
                    if h < HALVES - 1 and k in NEXT_SPLIT_AT:
                        split_x(h + 1, NEXT_SPLIT_AT[k])
            for c in range(MLP):
                dve.wait_ge(y_summed, c + 1)
                nc.vector.tensor_copy(y_sb[0:1, c * NB:(c + 1) * NB], y_ps(c)).then_inc(y_ready, 1)

        @block.tensor
        def _(pe):
            pe.wait_ge(consts_ready, 3)

            def transpose(h, a, first=False):
                pe.wait_ge(stage_gathered[a % 2], h * STAGE_INCS + (a // 2 + 1) * 2 * TILES * 16)
                for c in range(CH):
                    if not (first and c == 0):
                        pe.wait_ge(xt_ready, (h * STAGES + a) * CH + c)
                    for t in range(NB // P):
                        last = nc.tensor.transpose(
                            tr[:, t * P:(t + 1) * P],
                            gathered[:, a % 2, c * (NB // P) + t, :, :].rearrange("p f d -> p (f d)"), ident[:])
                    last.then_inc(transposed, 1)

            for a in range(AHEAD):
                transpose(0, a, first=(a == 0))
            for h in range(HALVES):
                def multiply(k):
                    u, s = h * NU + UNIT_OF[k], SLOTS[k][0]
                    if u % KB == 0:
                        pe.wait_ge(k_ready, u // KB + 1)
                    if SLOTS[k - 1][1] is None:
                        pe.wait_ge(split_loaded[s % 4], h * (32 * F // 4) + 32 * (s // 4 + 1))
                    if u >= MR:
                        pe.wait_ge(prod_ready, u - MR + 1)
                    cols = slice((u % KB) * P, (u % KB + 1) * P)
                    for part, k_part in enumerate((k_high, k_low)):
                        for c in range(CH):
                            last = nc.tensor.matmul(m_ps[:, u % MR, c * NB:(c + 1) * NB], k_part[:, u // KB % 4, cols],
                                                    x_split[:, s % 4, c * NB:(c + 1) * NB],
                                                    start=(part == 0), stop=(part == 1))
                    last.then_inc(unit_done, 1)

                def reduce(t):
                    b, q = divmod(t, BLOCK // 2)
                    if q == 0:
                        if h or b:
                            pe.wait_ge(z_ready, h * BLOCKS + b)
                    for k in (2 * t, 2 * t + 1):
                        s, m = SLOTS[k]
                        if m is None:
                            pe.wait_ge(split_loaded[s % 4], h * (32 * F // 4) + 32 * (s // 4 + 1))
                            data = x_split[:, s % 4, :].bitcast(fp32)
                        else:
                            pe.wait_ge(prod_ready, h * NU + UNIT_OF[k] + 1)
                            data = prod[:, (h * NU + UNIT_OF[k]) % PR, :]
                        for c in range(CH):
                            g = (k % 2) * 2 + c
                            last = nc.tensor.matmul(acc[g * BLOCK:(g + 1) * BLOCK, :],
                                                    sel[:, BLOCK - 2 - 2 * q:2 * BLOCK - 2 - 2 * q],
                                                    data[:, c * NB:(c + 1) * NB],
                                                    start=(q == 0), stop=(q == BLOCK // 2 - 1))
                    last.then_inc(reduced, 1)

                for k in range(NS):
                    if k in STAGE_AT:
                        transpose(h, STAGE_AT[k])
                    if k in NEXT_AT:
                        if h < HALVES - 1:
                            transpose(h + 1, NEXT_AT[k])
                    if k in UNIT_OF:
                        multiply(k)
                    if k % 2 == 0 and k > 2:
                        reduce(k // 2 - 2)
                reduce(REDUCES - 2)
                reduce(REDUCES - 1)

            pe.wait_ge(weights_loaded, 48)
            pe.wait_ge(small_loaded, 48)
            pe.wait_ge(prod_ready, HALVES * NU)
            pe.wait_ge(z_ready, HALVES * BLOCKS)
            pe.wait_ge(xt_ready, HALVES * CH * STAGES)

            def layer1(c):
                pe.wait_ge(z_loaded[c % 2], 48 * (c // 2 + 1))
                for n in range(H1 // P):
                    if c:
                        pe.wait_ge(h1_ready, (c - 1) * (H1 // P) + n + 1)
                    for kc in range(KC):
                        rows = P if kc < KC - 1 else KLAST
                        last = nc.tensor.matmul(h1_ps(c, n), w1_sb[0:rows, kc, n * P:(n + 1) * P],
                                                z_sb[0:rows, c % 2, kc, :], start=(kc == 0), stop=(kc == KC - 1))
                    last.then_inc(h1_summed, 1)

            def layer2(c):
                pe.wait_ge(h1_ready, (c + 1) * (H1 // P))
                for n in range(H2 // P):
                    if c:
                        pe.wait_ge(h2_ready, (c - 1) * (H2 // P) + n + 1)
                    for kc in range(H1 // P):
                        last = nc.tensor.matmul(h2_ps(c, n), w2_sb[:, kc, n * P:(n + 1) * P],
                                                h1_sb[:, c % 2, kc, :], start=(kc == 0), stop=(kc == H1 // P - 1))
                    last.then_inc(h2_summed, 1)

            def layer3(c):
                pe.wait_ge(h2_ready, (c + 1) * (H2 // P))
                if c >= 1:
                    pe.wait_ge(y_ready, c)
                for kc in range(H2 // P):
                    last = nc.tensor.matmul(y_ps(c), w3_sb[:, kc:kc + 1], h2_sb[:, c % 2, kc, :],
                                            start=(kc == 0), stop=(kc == H2 // P - 1))
                last.then_inc(y_summed, 1)

            layer1(0)
            for c in range(MLP):
                if c + 1 < MLP:
                    layer1(c + 1)
                layer2(c)
                layer3(c)


def kernel(**inputs):
    import numpy as np
    import concourse.bacc as bacc
    from concourse.bass_utils import run_bass_kernel_spmd

    ids = np.asarray(inputs["ids"])
    k_in = np.asarray(inputs["L0_rec_kernels"])
    w1_in = np.asarray(inputs["W_top1"])

    ids_l = ids.reshape(HALVES, TILES, P, STAGES, 2)[:, :, :, ::-1, :].transpose(0, 2, 3, 4, 1)
    k_l = np.zeros((D, NU, 2, D), k_in.dtype)
    w1_l = np.zeros((ZIN, H1), w1_in.dtype)
    for k, (s, m) in enumerate(SLOTS):
        i = F - 1 - s
        if m is None:
            w1_l[z_row(k, 0)] = w1_l[z_row(k, 1)] = w1_in[i]
            continue
        for t in range(2):
            if 2 * m + t > i:
                p = pair_index(i, 2 * m + t)
                k_l[:, UNIT_OF[k], t, :] = k_in[p]
                w1_l[z_row(k, t)] = w1_in[F + p]
    w1_l[ZROWS:] = w1_in[w1_in.shape[0] - DENSE:]

    arrays = {
        "ids": np.ascontiguousarray(ids_l).reshape(HALVES, P, F * TILES),
        "kmat": k_l.reshape(D, NU * P),
        "dense_t": np.ascontiguousarray(np.asarray(inputs["dense_ctx"]).T),
        "w1": w1_l,
        "b1": np.ascontiguousarray(np.asarray(inputs["b_top1"]).reshape(H1 // P, P).T),
        "w2": np.ascontiguousarray(inputs["W_top2"]),
        "b2": np.ascontiguousarray(np.asarray(inputs["b_top2"]).reshape(H2 // P, P).T),
        "w3": np.ascontiguousarray(np.asarray(inputs["W_top3"]).reshape(H2 // P, P).T),
    }
    for f in range(F):
        arrays[f"tbl_{f}"] = np.ascontiguousarray(inputs[f"tbl_{f}"])

    nc = bacc.Bacc("TRN2", target_bir_lowering=False, num_devices=1)
    aps = {name: nc.dram_tensor(f"in_{name}", a.shape, mybir.dt.from_np(a.dtype), kind="ExternalInput").ap()
           for name, a in arrays.items()}
    out = nc.dram_tensor("out_y", (1, B), mybir.dt.float32, kind="ExternalOutput").ap()
    dlrm_tower(nc, aps["ids"], [aps[f"tbl_{f}"] for f in range(F)], aps["kmat"], aps["dense_t"],
               aps["w1"], aps["b1"], aps["w2"], aps["b2"], aps["w3"], out)
    r = run_bass_kernel_spmd(nc, [{f"in_{n}": a for n, a in arrays.items()}], core_ids=[0])
    return np.asarray(r.results[0]["out_y"]).reshape(B, 1)
```

```python
from contextlib import ExitStack

import concourse.bass as bass
from concourse import mybir

B, F, D = 2048, 32, 64
DENSE, H1, H2 = 16, 512, 256
HALVES = 2
HB = B // HALVES
NB = 512
CH = HB // NB
TILES = HB // 128
STAGES = F // 2
MR = 3
PR = 5
P = 128


def pair_index(i, j):
    return i * F - i * (i + 1) // 2 + j - i - 1


def make_slots():
    slots = []
    for s in range(F):
        i = F - 1 - s
        if s % 2 == 0:
            slots.append((s, None))
        slots += [(s, m) for m in range(F // 2 - 1, (i + 1) // 2 - 1, -1)]
    return slots


SLOTS = make_slots()
NS = len(SLOTS)
UNITS = [(s, m) for s, m in SLOTS if m is not None]
NU = len(UNITS)
UNIT_OF = {}
SLOT_OF = []
for _k, (_s, _m) in enumerate(SLOTS):
    if _m is not None:
        UNIT_OF[_k] = len(SLOT_OF)
        SLOT_OF.append(_k)
FIRST = [[t for t, _ in SLOTS].index(s) for s in range(F)]
UNITS_UPTO = [sum(1 for s, _ in UNITS if s <= t) for t in range(F)]
BLOCK = 32
BLOCKS = (NS + BLOCK - 1) // BLOCK
ZROWS = 2 * NS
ZIN = ZROWS + DENSE
KC = (ZIN + P - 1) // P
KLAST = ZIN - (KC - 1) * P
KB = 4
KBATCH = NU // KB
KLEAD = 2
KLOAD = 3
REDUCES = NS // 2


def block_size(b):
    return min(BLOCK, NS - b * BLOCK)


def first(S):
    return S // F * NS + FIRST[S % F]


AHEAD = 2
TRANSPOSE_AT = {}
STAGE_SLOT = {}
for _G in range(AHEAD, HALVES * STAGES):
    _k = min(first(2 * _G - 1), 12 * _G - 21) if _G < STAGES else NS - 94 + 18 * (_G - STAGES)
    STAGE_SLOT[_G] = _k
    for _c in range(CH):
        TRANSPOSE_AT.setdefault(_k + _c, []).append((_G, _c))
SPLIT_AT, STACK_AT = {}, {}
for _G in range(AHEAD, HALVES * STAGES):
    _k = min(max(STAGE_SLOT[_G] + 3, first(2 * _G - 3)), first(2 * _G) - 1)
    SPLIT_AT.setdefault(_k, []).append(_G)
    STACK_AT.setdefault(min(_k + 2, first(2 * _G)), []).append(2 * _G)
    STACK_AT.setdefault(max(min(_k + 2, first(2 * _G)), first(2 * _G - 2)), []).append(2 * _G + 1)
GATHERS = 2 * TILES
GATHER_AT = {}
for _G in range(AHEAD, HALVES * STAGES):
    for _n in range(GATHERS):
        _k = STAGE_SLOT[_G - 2] + CH if _G - 2 >= AHEAD else 0
        GATHER_AT.setdefault(_k + (_n if _G >= STAGES else 0), []).append((_G, _n))
POOL_K = 42


def k_batches(h, k, lead):
    if k not in UNIT_OF or UNIT_OF[k] % KB:
        return ()
    g = h * KBATCH + UNIT_OF[k] // KB + lead
    return (g,) if g < HALVES * KBATCH else ()


def units_upto(S):
    return S // F * NU + UNITS_UPTO[S % F]


def reduces_of_unit(g):
    return (g // NU * NS + SLOT_OF[g % NU]) // 2 + 1


def z_row(k, t):
    b, kk = divmod(k, BLOCK)
    return b * 2 * BLOCK + (kk % 2) * block_size(b) + 2 * (kk // 2) + t


def dlrm_tower(nc, ids, tables, kmat, dense_t, w1, b1, w2, b2, w3, out):
    fp32, fp32r, i32 = mybir.dt.float32, mybir.dt.float32r, mybir.dt.int32
    ALU = mybir.AluOpType
    ACT = mybir.ActivationFunctionType

    z_dram = nc.dram_tensor("z_scratch", (ZROWS, B), fp32).ap()

    ctx = ExitStack()
    with ctx:
        def sb(name, shape, dt=fp32):
            return ctx.enter_context(nc.sbuf_tensor(name, shape, dt))

        def pb(name, shape, dt=fp32):
            return ctx.enter_context(nc.psum_tensor(name, shape, dt))

        def sem(name):
            return ctx.enter_context(nc.semaphore(name))

        x_t = sb("x_t", [P, HALVES, STAGES, HB])
        idx = sb("idx", [P, HALVES, F * TILES], i32)
        gathered = sb("gathered", [P, 2, TILES, 2, D])
        x_high = sb("x_high", [P, HB], fp32r)
        x_low = sb("x_low", [P, HB], fp32r)
        x_split = sb("x_split", [P, 4, HB], fp32r)
        k_raw = sb("k_raw", [P, 2, KB * P])
        k_high = sb("k_high", [P, 4, KB * P], fp32r)
        k_low = sb("k_low", [P, 4, KB * P], fp32r)
        prod = sb("prod", [P, PR, HB])
        z_out = sb("z_out", [P, 2, NB])
        ident = sb("ident", [P, P])
        sel = sb("sel", [P, 2 * BLOCK - 2])
        b1_sb = sb("b1_sb", [P, H1 // P])
        b2_sb = sb("b2_sb", [P, H2 // P])
        w3_sb = sb("w3_sb", [P, H2 // P])

        room = x_t[:, 0, :, :].rearrange("p a b -> p (a b)")
        at = [0]

        def take(n):
            at[0] += n
            assert at[0] <= STAGES * HB
            return room[:, at[0] - n:at[0]]

        w1_sb = take(KC * H1).rearrange("p (k n) -> p k n", k=KC)
        w2_sb = take(H1 // P * H2).rearrange("p (k n) -> p k n", k=H1 // P)
        z_sb = take(2 * KC * NB).rearrange("p (r k n) -> p r k n", r=2, k=KC)
        h1_sb = take(2 * (H1 // P) * NB).rearrange("p (r k n) -> p r k n", r=2, k=H1 // P)
        h2_sb = take(2 * (H2 // P) * NB).rearrange("p (r k n) -> p r k n", r=2, k=H2 // P)

        y_sb = gathered[0:1, :, :, :, :].rearrange("p a t f d -> p (a t f d)")[:, 0:B]

        m_ps = pb("m_ps", [P, MR, HB])
        acc = pb("acc", [P, NB])
        tr = pb("tr", [P, NB])

        consts_ready = sem("consts_ready")
        zeroed = sem("zeroed")
        sel_zeroed = sem("sel_zeroed")
        idx_loaded = sem("idx_loaded")
        stage_gathered = [sem(f"stage_gathered{r}") for r in range(2)]
        transposed = sem("transposed")
        xt_ready = sem("xt_ready")
        split_loaded = [sem(f"split_loaded{r}") for r in range(4)]
        x_high_ready = sem("x_high_ready")
        x_ready = sem("x_ready")
        k_loaded = [sem(f"k_loaded{r}") for r in range(2)]
        k_high_ready = sem("k_high_ready")
        k_ready = sem("k_ready")
        k_ready_pool = sem("k_ready_pool")
        unit_done = sem("unit_done")
        prod_ready = sem("prod_ready")
        reduced = sem("reduced")
        z_ready = sem("z_ready")
        z_stored = [sem(f"z_stored{r}") for r in range(2)]
        small_loaded = sem("small_loaded")
        weights_loaded = sem("weights_loaded")
        z_loaded = [sem(f"z_loaded{r}") for r in range(2)]
        h1_ready = sem("h1_ready")
        h2_ready = sem("h2_ready")
        y_summed = sem("y_summed")
        y_ready = sem("y_ready")
        y_stored = sem("y_stored")

        MLP = B // NB
        STORES = [len(range(r, BLOCKS, 2)) for r in range(2)]

        h1_summed = sem("h1_summed")
        h2_summed = sem("h2_summed")

        def h1_ps(c, n):
            return m_ps[:, n // 2, (n % 2) * NB:(n % 2 + 1) * NB]

        def h2_ps(c, n):
            return m_ps[:, 2, n * NB:(n + 1) * NB]

        def y_ps(c):
            return tr[0:1, :]

        def wait_k(engine, g):
            if g < POOL_K:
                engine.wait_ge(k_ready, g + 1)
            else:
                engine.wait_ge(k_ready_pool, g - POOL_K + 1)

        block = ctx.enter_context(nc.Block())

        @block.gpsimd
        def _(pool):
            nc.gpsimd.memset(ident[:], 0.0).then_inc(zeroed, 1)
            pool.wait_ge(zeroed, 1)
            nc.gpsimd.affine_select(out=ident[:], in_=ident[:], compare_op=ALU.not_equal, fill=1.0,
                                    base=0, pattern=[[-1, P]], channel_multiplier=1).then_inc(consts_ready, 1)

            pool.dma_start(idx[:], ids.rearrange("h p n -> p h n")).then_inc(idx_loaded, 16)
            pool.wait_ge(idx_loaded, 16)

            def gather(G, n):
                h, a = divmod(G, STAGES)
                t, f = divmod(n, 2)
                if n == 0 and G >= 2:
                    pool.wait_ge(transposed, (G - 1) * CH)
                col = (2 * a + f) * TILES + t
                nc.gpsimd.indirect_dma_start(
                    out=gathered[:, a % 2, t, f, :], out_offset=None, in_=tables[2 * (STAGES - 1 - a) + f],
                    in_offset=bass.IndirectOffsetOnAxis(ap=idx[:, h, col:col + 1], axis=0),
                ).then_inc(stage_gathered[a % 2], 16)

            def split_k(g):
                pool.wait_ge(k_high_ready, g + 1)
                nc.gpsimd.tensor_tensor(k_low[:, g % 4, :], k_raw[:, g % 2, :],
                                        k_high[:, g % 4, :].bitcast(fp32), ALU.subtract).then_inc(k_ready_pool, 1)

            for G in range(AHEAD):
                for n in range(GATHERS):
                    gather(G, n)
            for h in range(HALVES):
                for k in range(NS):
                    for g in k_batches(h, k, KLEAD):
                        if g >= POOL_K:
                            split_k(g)
                    for G, n in GATHER_AT.get(h * NS + k, ()):
                        gather(G, n)

        @block.sync
        def _(sp):
            sp.dma_start(b1_sb[:], b1).then_inc(small_loaded, 16)
            sp.dma_start(b2_sb[:], b2).then_inc(small_loaded, 16)
            sp.dma_start(w3_sb[:], w3).then_inc(small_loaded, 16)

            def load_weights():
                sp.wait_ge(x_ready, STAGES)
                sp.wait_ge(reduced, REDUCES)
                sp.wait_ge(prod_ready, NU)
                sp.dma_start(w1_sb[:, 0:KC - 1, :], w1[0:(KC - 1) * P, :].rearrange("(k p) n -> p k n", p=P)).then_inc(weights_loaded, 16)
                sp.dma_start(w1_sb[0:KLAST, KC - 1, :], w1[(KC - 1) * P:ZIN, :]).then_inc(weights_loaded, 16)
                sp.dma_start(w2_sb, w2.rearrange("(k p) n -> p k n", p=P)).then_inc(weights_loaded, 16)

            def load_z(c):
                if c >= 2:
                    sp.wait_ge(h1_summed, (c - 1) * (H1 // P))
                if c % CH == 0:
                    for r in range(2):
                        sp.wait_ge(z_stored[r], (c // CH + 1) * STORES[r] * 64)
                cols = slice(c * NB, (c + 1) * NB)
                sp.dma_start(z_sb[:, c % 2, 0:KC - 1, :],
                             z_dram[0:(KC - 1) * P, cols].rearrange("(k p) n -> p k n", p=P)).then_inc(z_loaded[c % 2], 16)
                sp.dma_start(z_sb[0:KLAST - DENSE, c % 2, KC - 1, :], z_dram[(KC - 1) * P:ZROWS, cols]).then_inc(z_loaded[c % 2], 16)
                sp.dma_start(z_sb[KLAST - DENSE:KLAST, c % 2, KC - 1, :], dense_t[:, cols]).then_inc(z_loaded[c % 2], 16)

            for h in range(HALVES):
                def load_k(g):
                    if g >= 2:
                        wait_k(sp, g - 2)
                    kb = g % KBATCH
                    for half in range(2):
                        sp.dma_start(k_raw[half * D:half * D + D, g % 2, :],
                                     kmat[:, kb * KB * P:(kb + 1) * KB * P]).then_inc(k_loaded[g % 2], 16)

                def stack_x(S):
                    a, lo, r = S // 2, (F - 1 - S) % 2 * D, S % 4
                    if S >= 4:
                        sp.wait_ge(unit_done, units_upto(S - 4))
                    sp.wait_ge(x_ready, a + 1)
                    sp.dma_start(x_split[0:D, r, :].bitcast(fp32), x_high[lo:lo + D, :].bitcast(fp32)).then_inc(split_loaded[r], 16)
                    sp.dma_start(x_split[D:P, r, :].bitcast(fp32), x_low[lo:lo + D, :].bitcast(fp32)).then_inc(split_loaded[r], 16)

                def store_z(b):
                    sp.wait_ge(z_ready, h * BLOCKS + b + 1)
                    n = block_size(b)
                    for g in range(4):
                        row = b * 2 * BLOCK + (g // 2) * n
                        col = h * HB + (g % 2) * NB
                        sp.dma_start(z_dram[row:row + n, col:col + NB],
                                     z_out[g * BLOCK:g * BLOCK + n, b % 2, :]).then_inc(z_stored[b % 2], 16)

                if h == 0:
                    for kb in range(KLOAD):
                        load_k(kb)
                    for S in range(2 * AHEAD):
                        stack_x(S)
                for k in range(NS):
                    if h and k == NS // 2:
                        load_weights()
                        load_z(0)
                        load_z(1)
                    for S in STACK_AT.get(h * NS + k, ()):
                        stack_x(S)
                    for g in k_batches(h, k, KLOAD):
                        load_k(g)
                    if k % BLOCK == 6 and k > BLOCK:
                        store_z(k // BLOCK - 1)
                store_z(BLOCKS - 1)
            for c in range(2, MLP):
                load_z(c)
            sp.wait_ge(y_ready, MLP)
            sp.dma_start(out, y_sb).then_inc(y_stored, 16)
            sp.wait_ge(y_stored, 16)

        @block.scalar
        def _(act):
            def keep_xt(G, c):
                act.wait_ge(transposed, G * CH + c + 1)
                nc.scalar.activation(x_t[:, G // STAGES, G % STAGES, c * NB:(c + 1) * NB], tr[:], ACT.Copy).then_inc(xt_ready, 1)

            for G in range(AHEAD):
                for c in range(CH):
                    keep_xt(G, c)
            for h in range(HALVES):
                def split_k(g):
                    act.wait_ge(k_loaded[g % 2], 32 * (g // 2 + 1))
                    if g >= 4:
                        act.wait_ge(unit_done, KB * (g - 3))
                    nc.scalar.activation(k_high[:, g % 4, :], k_raw[:, g % 2, :], ACT.Copy).then_inc(k_high_ready, 1)

                def split_x(G):
                    for S in (2 * G - 2, 2 * G - 1) if G else ():
                        act.wait_ge(split_loaded[S % 4], 32 * (S // 4 + 1))
                    act.wait_ge(xt_ready, (G + 1) * CH)
                    nc.scalar.activation(x_high[:], x_t[:, G // STAGES, G % STAGES, :], ACT.Copy).then_inc(x_high_ready, 1)

                def keep_z(b):
                    act.wait_ge(reduced, h * REDUCES + (b * BLOCK + block_size(b)) // 2)
                    if h or b >= 2:
                        act.wait_ge(z_stored[b % 2], h * (64 * STORES[b % 2]) + 64 * (b // 2))
                    nc.scalar.activation(z_out[:, b % 2, :], acc[:], ACT.Copy).then_inc(z_ready, 1)

                if h == 0:
                    split_x(0)
                    for g in range(KLEAD):
                        split_k(g)
                    split_x(1)
                for k in range(NS):
                    for G, c in TRANSPOSE_AT.get(h * NS + k, ()):
                        keep_xt(G, c)
                    for G in SPLIT_AT.get(h * NS + k, ()):
                        split_x(G)
                    for g in k_batches(h, k, KLEAD):
                        split_k(g)
                    if k % BLOCK == 3 and k > BLOCK:
                        keep_z(k // BLOCK - 1)
                keep_z(BLOCKS - 1)
            act.wait_ge(small_loaded, 48)

            def keep_h1(c):
                if c >= 2:
                    act.wait_ge(h2_summed, (c - 1) * (H2 // P))
                for n in range(H1 // P):
                    act.wait_ge(h1_summed, c * (H1 // P) + n + 1)
                    last = nc.scalar.activation(h1_sb[:, c % 2, n, :], h1_ps(c, n), ACT.Relu,
                                                bias=b1_sb[:, n:n + 1])
                    last.then_inc(h1_ready, 1)

            def keep_h2(c):
                if c >= 2:
                    act.wait_ge(y_summed, c - 1)
                for n in range(H2 // P):
                    act.wait_ge(h2_summed, c * (H2 // P) + n + 1)
                    nc.scalar.activation(h2_sb[:, c % 2, n, :], h2_ps(c, n), ACT.Relu,
                                         bias=b2_sb[:, n:n + 1]).then_inc(h2_ready, 1)

            keep_h1(0)
            for c in range(MLP):
                if c + 1 < MLP:
                    keep_h1(c + 1)
                keep_h2(c)

        @block.vector
        def _(dve):
            nc.vector.memset(sel[:], 0.0).then_inc(sel_zeroed, 1)
            dve.wait_ge(sel_zeroed, 1)
            nc.vector.memset(sel[0:D, BLOCK - 2:BLOCK - 1], 1.0).then_inc(consts_ready, 1)
            nc.vector.memset(sel[D:P, BLOCK - 1:BLOCK], 1.0).then_inc(consts_ready, 1)
            for h in range(HALVES):
                def split_k(g):
                    dve.wait_ge(k_high_ready, g + 1)
                    nc.vector.tensor_tensor(k_low[:, g % 4, :], k_raw[:, g % 2, :],
                                            k_high[:, g % 4, :].bitcast(fp32), ALU.subtract).then_inc(k_ready, 1)

                def split_x(G):
                    dve.wait_ge(x_high_ready, G + 1)
                    nc.vector.tensor_tensor(x_low[:], x_t[:, G // STAGES, G % STAGES, :],
                                            x_high[:].bitcast(fp32), ALU.subtract).then_inc(x_ready, 1)

                if h == 0:
                    split_x(0)
                    for g in range(KLEAD):
                        split_k(g)
                    split_x(1)
                for k in range(NS):
                    if k in UNIT_OF:
                        u, m = h * NU + UNIT_OF[k], SLOTS[k][1]
                        dve.wait_ge(unit_done, u + 1)
                        if u >= PR:
                            dve.wait_ge(reduced, reduces_of_unit(u - PR))
                        nc.vector.tensor_tensor(prod[:, u % PR, :], m_ps[:, u % MR, :],
                                                x_t[:, h, STAGES - 1 - m, :], ALU.mult).then_inc(prod_ready, 1)
                        for g in k_batches(h, k, KLEAD):
                            if g < POOL_K:
                                split_k(g)
                    for G in SPLIT_AT.get(h * NS + k, ()):
                        split_x(G)
            for c in range(MLP):
                dve.wait_ge(y_summed, c + 1)
                nc.vector.tensor_copy(y_sb[0:1, c * NB:(c + 1) * NB], y_ps(c)).then_inc(y_ready, 1)

        @block.tensor
        def _(pe):
            pe.wait_ge(consts_ready, 3)

            def transpose(G, c):
                if c == 0:
                    pe.wait_ge(stage_gathered[G % 2], (G // 2 + 1) * GATHERS * 16)
                if G or c:
                    pe.wait_ge(xt_ready, G * CH + c)
                for t in range(NB // P):
                    last = nc.tensor.transpose(
                        tr[:, t * P:(t + 1) * P],
                        gathered[:, G % 2, c * (NB // P) + t, :, :].rearrange("p f d -> p (f d)"), ident[:])
                last.then_inc(transposed, 1)

            for G in range(AHEAD):
                for c in range(CH):
                    transpose(G, c)
            for h in range(HALVES):
                def multiply(k):
                    u, s = h * NU + UNIT_OF[k], SLOTS[k][0]
                    if u % KB == 0:
                        wait_k(pe, u // KB)
                    if SLOTS[k - 1] != (s, SLOTS[k][1] + 1):
                        pe.wait_ge(split_loaded[s % 4], h * (32 * F // 4) + 32 * (s // 4 + 1))
                    if u >= MR:
                        pe.wait_ge(prod_ready, u - MR + 1)
                    cols = slice((u % KB) * P, (u % KB + 1) * P)
                    for part, k_part in enumerate((k_high, k_low)):
                        for c in range(CH):
                            last = nc.tensor.matmul(m_ps[:, u % MR, c * NB:(c + 1) * NB], k_part[:, u // KB % 4, cols],
                                                    x_split[:, s % 4, c * NB:(c + 1) * NB],
                                                    start=(part == 0), stop=(part == 1))
                    last.then_inc(unit_done, 1)

                def reduce(t):
                    b, q = divmod(t, BLOCK // 2)
                    if q == 0:
                        if h or b:
                            pe.wait_ge(z_ready, h * BLOCKS + b)
                    for k in (2 * t, 2 * t + 1):
                        s, m = SLOTS[k]
                        if m is None:
                            pe.wait_ge(xt_ready, (h * STAGES + s // 2 + 1) * CH)
                            data = x_t[:, h, s // 2, :]
                        else:
                            pe.wait_ge(prod_ready, h * NU + UNIT_OF[k] + 1)
                            data = prod[:, (h * NU + UNIT_OF[k]) % PR, :]
                        for c in range(CH):
                            g = (k % 2) * 2 + c
                            last = nc.tensor.matmul(acc[g * BLOCK:(g + 1) * BLOCK, :],
                                                    sel[:, BLOCK - 2 - 2 * q:2 * BLOCK - 2 - 2 * q],
                                                    data[:, c * NB:(c + 1) * NB],
                                                    start=(q == 0), stop=(q == block_size(b) // 2 - 1))
                    last.then_inc(reduced, 1)

                for k in range(NS):
                    for G, c in TRANSPOSE_AT.get(h * NS + k, ()):
                        transpose(G, c)
                    if k in UNIT_OF:
                        multiply(k)
                    if k % 2 == 0 and k > 2:
                        reduce(k // 2 - 2)
                reduce(REDUCES - 2)
                reduce(REDUCES - 1)

            pe.wait_ge(weights_loaded, 48)
            pe.wait_ge(small_loaded, 48)
            pe.wait_ge(prod_ready, HALVES * NU)
            pe.wait_ge(z_ready, HALVES * BLOCKS)
            pe.wait_ge(xt_ready, HALVES * CH * STAGES)

            def layer1(c):
                pe.wait_ge(z_loaded[c % 2], 48 * (c // 2 + 1))
                for n in range(H1 // P):
                    if c:
                        pe.wait_ge(h1_ready, (c - 1) * (H1 // P) + n + 1)
                    for kc in range(KC):
                        rows = P if kc < KC - 1 else KLAST
                        last = nc.tensor.matmul(h1_ps(c, n), w1_sb[0:rows, kc, n * P:(n + 1) * P],
                                                z_sb[0:rows, c % 2, kc, :], start=(kc == 0), stop=(kc == KC - 1))
                    last.then_inc(h1_summed, 1)

            def layer2(c):
                pe.wait_ge(h1_ready, (c + 1) * (H1 // P))
                for n in range(H2 // P):
                    if c:
                        pe.wait_ge(h2_ready, (c - 1) * (H2 // P) + n + 1)
                    for kc in range(H1 // P):
                        last = nc.tensor.matmul(h2_ps(c, n), w2_sb[:, kc, n * P:(n + 1) * P],
                                                h1_sb[:, c % 2, kc, :], start=(kc == 0), stop=(kc == H1 // P - 1))
                    last.then_inc(h2_summed, 1)

            def layer3(c):
                pe.wait_ge(h2_ready, (c + 1) * (H2 // P))
                if c >= 1:
                    pe.wait_ge(y_ready, c)
                for kc in range(H2 // P):
                    last = nc.tensor.matmul(y_ps(c), w3_sb[:, kc:kc + 1], h2_sb[:, c % 2, kc, :],
                                            start=(kc == 0), stop=(kc == H2 // P - 1))
                last.then_inc(y_summed, 1)

            layer1(0)
            for c in range(MLP):
                if c + 1 < MLP:
                    layer1(c + 1)
                layer2(c)
                layer3(c)


def kernel(**inputs):
    import numpy as np
    import concourse.bacc as bacc
    from concourse.bass_utils import run_bass_kernel_spmd

    ids = np.asarray(inputs["ids"])
    k_in = np.asarray(inputs["L0_rec_kernels"])
    w1_in = np.asarray(inputs["W_top1"])

    ids_l = ids.reshape(HALVES, TILES, P, STAGES, 2)[:, :, :, ::-1, :].transpose(0, 2, 3, 4, 1)
    k_l = np.zeros((D, NU, 2, D), k_in.dtype)
    w1_l = np.zeros((ZIN, H1), w1_in.dtype)
    for k, (s, m) in enumerate(SLOTS):
        i = F - 1 - s
        if m is None:
            w1_l[z_row(k, 0)], w1_l[z_row(k, 1)] = w1_in[i - 1], w1_in[i]
            continue
        for t in range(2):
            if 2 * m + t > i:
                p = pair_index(i, 2 * m + t)
                k_l[:, UNIT_OF[k], t, :] = k_in[p]
                w1_l[z_row(k, t)] = w1_in[F + p]
    w1_l[ZROWS:] = w1_in[w1_in.shape[0] - DENSE:]

    arrays = {
        "ids": np.ascontiguousarray(ids_l).reshape(HALVES, P, F * TILES),
        "kmat": k_l.reshape(D, NU * P),
        "dense_t": np.ascontiguousarray(np.asarray(inputs["dense_ctx"]).T),
        "w1": w1_l,
        "b1": np.ascontiguousarray(np.asarray(inputs["b_top1"]).reshape(H1 // P, P).T),
        "w2": np.ascontiguousarray(inputs["W_top2"]),
        "b2": np.ascontiguousarray(np.asarray(inputs["b_top2"]).reshape(H2 // P, P).T),
        "w3": np.ascontiguousarray(np.asarray(inputs["W_top3"]).reshape(H2 // P, P).T),
    }
    for f in range(F):
        arrays[f"tbl_{f}"] = np.ascontiguousarray(inputs[f"tbl_{f}"])

    nc = bacc.Bacc("TRN2", target_bir_lowering=False, num_devices=1)
    aps = {name: nc.dram_tensor(f"in_{name}", a.shape, mybir.dt.from_np(a.dtype), kind="ExternalInput").ap()
           for name, a in arrays.items()}
    out = nc.dram_tensor("out_y", (1, B), mybir.dt.float32, kind="ExternalOutput").ap()
    dlrm_tower(nc, aps["ids"], [aps[f"tbl_{f}"] for f in range(F)], aps["kmat"], aps["dense_t"],
               aps["w1"], aps["b1"], aps["w2"], aps["b2"], aps["w3"], out)
    r = run_bass_kernel_spmd(nc, [{f"in_{n}": a for n, a in arrays.items()}], core_ids=[0])
    return np.asarray(r.results[0]["out_y"]).reshape(B, 1)
```
